# Optimizing a Trainium2 kernel written in Bass

```python
import numpy as np
import jax
import jax.numpy as jnp

def _softmax(x, axis=-1):
    return jax.nn.softmax(x, axis=axis)

def _gelu(x):
    return jax.nn.gelu(x, approximate=True)

def _silu(x):
    return jax.nn.silu(x)

def _sigmoid(x):
    return jax.nn.sigmoid(x)

def _layernorm(x, axis=-1, eps=1e-05):
    m = jnp.mean(x, axis=axis, keepdims=True)
    v = jnp.var(x, axis=axis, keepdims=True)
    return (x - m) / jnp.sqrt(v + eps)

def _scatter_add(tgt, idx, src, axis=0):
    return tgt.at[idx].add(src)

def _segment_sum(src, seg, n):
    return jax.ops.segment_sum(src, seg, n)
kernel_name = 'mk_rec_standalone_d1_rec_r8_756f7b'

def setup_inputs(seed: int=0):
    np.random.seed(seed)
    _w = jnp.asarray

    def _rec_inputs():
        import jax
        import jax.numpy as jnp
        _rk = jax.random.key(seed)
        r_x = -7.10856e-05 + 0.999911 * jax.random.normal(jax.random.fold_in(_rk, 1), (512, 512, 64), jnp.float32)
        return r_x
    r_x = _rec_inputs()

    def _L0_rec_setup():
        import jax, jax.numpy as jnp
        import numpy as np
        B, DIM, C = (256, 512, 64)
        INTER = DIM // 4
        EPS = 1e-05
        key = jax.random.key(seed)
        ks = jax.random.split(key, 14)

        def n(k, shape, scale=0.05):
            return jax.random.normal(k, shape, dtype=jnp.float32) * scale
        return {'x': jax.random.normal(ks[0], (B, DIM, C), dtype=jnp.float32), 'W1': n(ks[1], (C, INTER, DIM)), 'b1': n(ks[2], (C, INTER)), 'g1': 1.0 + n(ks[3], (C, INTER)), 'be1': n(ks[4], (C, INTER)), 'm1': n(ks[5], (C, INTER)), 'v1': jax.random.uniform(ks[6], (C, INTER), dtype=jnp.float32, minval=0.5, maxval=1.5), 'W2': n(ks[7], (C, DIM, INTER)), 'b2': n(ks[8], (C, DIM)), 'g2': 1.0 + n(ks[9], (C, DIM)), 'be2': n(ks[10], (C, DIM)), 'm2': n(ks[11], (C, DIM)), 'v2': jax.random.uniform(ks[12], (C, DIM), dtype=jnp.float32, minval=0.5, maxval=1.5)}
    _L0_rec_all = _L0_rec_setup()
    _L0_rec_in = {k: v for k, v in _L0_rec_all.items() if k in ('W1', 'b1', 'g1', 'be1', 'm1', 'v1', 'W2', 'b2', 'g2', 'be2', 'm2', 'v2')}
    del _L0_rec_all
    return {'r_x': r_x, 'L0_rec_W1': _L0_rec_in['W1'], 'L0_rec_b1': _L0_rec_in['b1'], 'L0_rec_g1': _L0_rec_in['g1'], 'L0_rec_be1': _L0_rec_in['be1'], 'L0_rec_m1': _L0_rec_in['m1'], 'L0_rec_v1': _L0_rec_in['v1'], 'L0_rec_W2': _L0_rec_in['W2'], 'L0_rec_b2': _L0_rec_in['b2'], 'L0_rec_g2': _L0_rec_in['g2'], 'L0_rec_be2': _L0_rec_in['be2'], 'L0_rec_m2': _L0_rec_in['m2'], 'L0_rec_v2': _L0_rec_in['v2']}

def reference(r_x, L0_rec_W1, L0_rec_b1, L0_rec_g1, L0_rec_be1, L0_rec_m1, L0_rec_v1, L0_rec_W2, L0_rec_b2, L0_rec_g2, L0_rec_be2, L0_rec_m2, L0_rec_v2):
    import jax
    import jax.numpy as jnp

    def _L0_rec_ref(x, W1, b1, g1, be1, m1, v1, W2, b2, g2, be2, m2, v2):
        import jax, jax.numpy as jnp
        import numpy as np
        B, DIM, C = (256, 512, 64)
        INTER = DIM // 4
        EPS = 1e-05
        h = jnp.einsum('bdc,cid->bci', x, W1) + b1[None]
        h = (h - m1[None]) * (g1[None] * jax.lax.rsqrt(v1 + EPS)[None]) + be1[None]
        h = jax.nn.relu(h)
        y = jnp.einsum('bci,cdi->bcd', h, W2) + b2[None]
        y = (y - m2[None]) * (g2[None] * jax.lax.rsqrt(v2 + EPS)[None]) + be2[None]
        w = jax.nn.sigmoid(jnp.transpose(y, (0, 2, 1)))
        return w
    y = _L0_rec_ref(r_x, L0_rec_W1, L0_rec_b1, L0_rec_g1, L0_rec_be1, L0_rec_m1, L0_rec_v1, L0_rec_W2, L0_rec_b2, L0_rec_g2, L0_rec_be2, L0_rec_m2, L0_rec_v2)
    return y

_drawn_inputs = setup_inputs


def setup_inputs(seed=0):
    import zlib

    import numpy as np

    out = dict(_drawn_inputs(seed))
    spreads = {}
    factors = {'L0_rec_b1': 5.659,
     'L0_rec_g1': 4.965,
     'L0_rec_be1': 5.899,
     'L0_rec_m1': 5.697,
     'L0_rec_g2': 200.0,
     'L0_rec_be2': 24.268,
     'L0_rec_v2': 21.836}
    for name, (base, spread) in spreads.items():
        noise = np.random.default_rng([zlib.crc32(name.encode()), seed]).standard_normal(out[name].shape)
        drawn = base * np.exp(spread * noise) if base else spread * noise
        out[name] = jnp.asarray(drawn.astype(out[name].dtype))
    for name, factor in factors.items():
        out[name] = (out[name] * factor).astype(out[name].dtype)
    return out
```

```python
import concourse.bass as bass
from concourse import mybir
from contextlib import ExitStack


def squeeze_expand_gate_kernel(nc, x, W1, b1, g1, be1, m1, v1, W2, b2, g2, be2, m2, v2, out):
    fp32, bf16 = mybir.dt.float32, mybir.dt.bfloat16
    ALU = mybir.AluOpType
    ACT = mybir.ActivationFunctionType
    P = nc.NUM_PARTITIONS
    EPS = 1e-5

    B, D, C = x.shape
    I = W1.shape[1]
    assert I == P and C % 16 == 0

    D1 = P
    CHUNKS1 = D // D1
    B1 = 64
    TILES1 = B // B1
    D2 = 64
    CHUNKS2 = D // D2
    B2 = P
    TILES2 = B // B2
    GC = 8
    GROUPS = C // GC
    BANK = 512
    assert GC * B1 == BANK and GC * D2 == BANK
    PAIRS = C // 2
    QP = 8
    LOTS2 = PAIRS // QP
    PARTS = 3

    MM_BANKS = 4
    PREP_BANKS = 4
    SLOTS = 3
    RAW = 2
    SLOT1 = [t % SLOTS for t in range(TILES1)]
    SLOT2 = [0, 1, 2, 1]
    assert TILES2 == len(SLOT2)
    ITEMS1 = 2 * GROUPS
    IC = GC // 2
    N_W1 = CHUNKS1 * ITEMS1
    N_G1 = CHUNKS1 * TILES1 * GROUPS
    G1, G2 = TILES1 * GROUPS, TILES2 * GROUPS
    LOTS1 = CHUNKS1 * GROUPS
    assert TILES1 >= 8 and LOTS1 % RAW == 0

    with ExitStack() as ctx:
        def sb(name, shape, dt=fp32):
            return ctx.enter_context(nc.sbuf_tensor(name, shape, dt))

        def sem(name):
            return ctx.enter_context(nc.semaphore(name))

        h = sb("h", [P, C, B])
        wt = sb("wt", [P, C * I])
        w1t = wt[:, :].rearrange("p (c i) -> p c i", c=C)
        w2t = wt[:, 0:C * D2].rearrange("p (c d) -> p c d", c=C)
        shifts = wt[:, C * D2:2 * C * D2].rearrange("p (g d c) -> p g d c", g=GROUPS, c=GC)
        slots = [sb(f"slot{s}", [P, B1 * C]) for s in range(SLOTS)]
        xt = [s[:, :].rearrange("p (b c) -> p b c", c=C) for s in slots]
        yt = [s[:, :].rearrange("p (d c) -> p d c", c=C) for s in slots]
        raw = [sb(f"raw{s}", [P, GC * D1]) for s in range(RAW)]
        raw1 = [r[:, :].rearrange("p (c d) -> p c d", d=D1) for r in raw]
        raw2 = [r[:, :].rearrange("p (c i) -> p c i", i=I) for r in raw]
        ident = sb("ident", [P, P])
        ones_at = sb("ones_at", [PARTS * PAIRS, PAIRS], bf16)
        s1t = sb("s1t", [P, C])
        t1t = sb("t1t", [P, C])
        s2t = sb("s2t", [P, CHUNKS2, PAIRS])
        t2p = sb("t2p", [PARTS * PAIRS, 2, D], bf16)

        TMP0 = 20
        tmp = h[:, TMP0:C, :].rearrange("p c b -> p (c b)")
        R1, R2 = C, PARTS * PAIRS
        E2 = 2 * D
        prm1 = [tmp[0:R1, k * I:(k + 1) * I] for k in range(5)]
        wk1 = [tmp[0:R1, (5 + k) * I:(6 + k) * I] for k in range(4)]
        OFF = 9 * I
        prm2 = [tmp[0:R2, OFF + k * E2:OFF + (k + 1) * E2] for k in range(5)]
        wk2 = [tmp[0:R2, OFF + (5 + k) * E2:OFF + (6 + k) * E2] for k in range(4)]
        part_bf = tmp[0:R2, OFF + 9 * E2:OFF + 9 * E2 + E2 // 2].bitcast(bf16)
        assert OFF + 10 * E2 <= (C - TMP0) * B

        scale1, shift1, scale2 = wk1[0], wk1[2], wk2[1]
        psum = [ctx.enter_context(nc.psum_tensor(f"bank{k}", [P, BANK], fp32))
                for k in range(MM_BANKS + PREP_BANKS)]
        mm_bank, prep_bank = psum[:MM_BANKS], psum[MM_BANKS:]

        ident_made = sem("ident_made")
        params_loaded = [sem(f"params{k}_loaded") for k in (1, 2)]
        dve_step = sem("dve_step")
        sqrt_asked = sem("sqrt_asked")
        sqrt_done = sem("sqrt_done")
        bn1_worked = sem("bn1_worked")
        bn2_worked = sem("bn2_worked")
        bn_turned = sem("bn_turned")
        bn1_ready = sem("bn1_ready")
        bn2_ready = sem("bn2_ready")
        x_loaded = [sem(f"x_loaded{s}") for s in range(SLOTS)]
        w1_loaded = [sem(f"w1_loaded{s}") for s in range(RAW)]
        w2_loaded = [sem(f"w2_loaded{s}") for s in range(RAW)]
        raw_scaled = sem("raw_scaled")
        prep_made = sem("prep_made")
        prep_copied = sem("prep_copied")
        spread_made = sem("spread_made")
        spread_copied = sem("spread_copied")
        group_made = sem("group_made")
        group_taken = sem("group_taken")
        relu_done = sem("relu_done")
        sigm_done = sem("sigm_done")
        stored = [sem(f"stored{s}") for s in range(SLOTS)]

        def taken(n):
            return n + MM_BANKS

        def group1(j, t, g):
            return G1 * j + (t * GROUPS + g + 1)

        def group2(k, t, g):
            return G2 * k + (N_G1 + t * GROUPS + g + 1)

        W2_pairs = W2.rearrange("(c two) d i -> two d c i", two=2)
        LAST = TILES1 - 1
        block = ctx.enter_context(nc.Block())

        @block.sync
        def _(sp):
            def load_x(j, t):
                sp.dma_start(xt[SLOT1[t]], x[t * B1:(t + 1) * B1, j * D1:(j + 1) * D1, :].rearrange("b d c -> d b c")
                             ).then_inc(x_loaded[SLOT1[t]], 16)

            def load_w1(j, q):
                sp.dma_start(raw1[q % RAW], W1[q * GC:(q + 1) * GC, :, j * D1:(j + 1) * D1].rearrange("c i d -> i c d")
                             ).then_inc(w1_loaded[q % RAW], 16)

            def load_w2(k, q):
                for two in range(2):
                    sp.dma_start(raw2[q % RAW][two * D2:(two + 1) * D2],
                                 W2_pairs[two, bass.ts(k, D2), q * QP:(q + 1) * QP, :]
                                 ).then_inc(w2_loaded[q % RAW], 16)

            def rest_of_chunk(j):
                for t in range(SLOTS, TILES1):
                    sp.wait_ge(group_made, group1(j, t - SLOTS, GROUPS - 1))
                    load_x(j, t)

            for q in range(GROUPS):
                if q >= RAW:
                    sp.wait_ge(prep_made, 2 * (q - RAW + 1))
                load_w1(0, q)
                if q == 1:
                    load_x(0, 0)
                if q == 3:
                    load_x(0, 1)
            load_x(0, 2)

            for j in range(CHUNKS1 - 1):
                rest_of_chunk(j)
                sp.wait_ge(prep_made, ITEMS1 * j + ITEMS1)
                for q in range(RAW):
                    load_w1(j + 1, q)
                sp.wait_ge(group_made, group1(j, LAST - 2, GROUPS - 1))
                load_x(j + 1, 2)
                sp.wait_ge(group_made, group1(j, LAST - 1, GROUPS - 1))
                load_x(j + 1, 0)
                for q in range(RAW, GROUPS):
                    sp.wait_ge(prep_made, ITEMS1 * j + (ITEMS1 + 2 * (q - RAW + 1)))
                    load_w1(j + 1, q)
                sp.wait_ge(group_made, group1(j, LAST, GROUPS - 1))
                load_x(j + 1, 1)
            rest_of_chunk(CHUNKS1 - 1)

            for q in range(LOTS2):
                sp.wait_ge(prep_made, N_W1 + 2 * (q - RAW + 1))
                load_w2(0, q)

            def store(k, t):
                sp.wait_ge(sigm_done, (G2 // 2) * k + (GROUPS // 2) * (t + 1))
                sp.dma_start(out[t * B2:(t + 1) * B2, bass.ts(k, D2), :], yt[SLOT2[t]]
                             ).then_inc(stored[SLOT2[t]], 16)

            with sp.Fori(0, CHUNKS2 - 1) as k:
                for t in range(TILES2):
                    if t == 0:
                        sp.wait_ge(prep_made, GROUPS * k + (N_W1 + GROUPS))
                        for q in range(RAW):
                            load_w2(k + 1, q)
                    if t == TILES2 - 1:
                        for q in range(RAW, LOTS2):
                            sp.wait_ge(prep_made, GROUPS * k + (N_W1 + GROUPS + 2 * (q - RAW + 1)))
                            load_w2(k + 1, q)
                    store(k, t)
            for t in range(TILES2):
                store(CHUNKS2 - 1, t)
            for s in range(SLOTS):
                sp.wait_ge(stored[s], 16 * CHUNKS2 * SLOT2.count(s))

        @block.gpsimd
        def _(pool):
            nc.gpsimd.memset(ident[:, :], 0.0).then_inc(ident_made, 1)
            pool.wait_ge(ident_made, 1)
            nc.gpsimd.affine_select(out=ident[:, :], in_=ident[:, :], compare_op=ALU.not_equal, fill=1.0,
                                    base=0, pattern=[[-1, P]], channel_multiplier=1).then_inc(ident_made, 1)
            pool.wait_ge(bn1_ready, 1)
            for n in range(LOTS1):
                q = n % GROUPS
                pool.wait_ge(w1_loaded[n % RAW], 16 * (n // RAW + 1))
                r = raw1[n % RAW]
                scale = s1t[:, q * GC:(q + 1) * GC].unsqueeze(2).to_broadcast([P, GC, D1])
                nc.gpsimd.tensor_tensor(r, r, scale, ALU.mult).then_inc(raw_scaled, 1)
            pool.wait_ge(bn2_ready, 1)
            for n in range(CHUNKS2 * LOTS2):
                k, q = n // LOTS2, n % LOTS2
                pool.wait_ge(w2_loaded[n % RAW], 32 * (n // RAW + 1))
                r = raw2[n % RAW]
                scale = s2t[:, k, q * QP:(q + 1) * QP].unsqueeze(2).to_broadcast([P, QP, I])
                nc.gpsimd.tensor_tensor(r, r, scale, ALU.mult).then_inc(raw_scaled, 1)

        @block.tensor
        def _(pe):
            pe.wait_ge(ident_made, 2)
            pe.wait_ge(bn1_worked, 1)
            nc.tensor.transpose(mm_bank[0][:, 0:C], scale1, ident[0:R1, 0:R1])
            nc.tensor.transpose(mm_bank[0][:, C:2 * C], shift1, ident[0:R1, 0:R1]).then_inc(bn_turned, 1)

            def prep_w1(j, q, first=False):
                pe.wait_ge(raw_scaled, GROUPS * j + (q + 1))
                for m in (2 * q, 2 * q + 1):
                    if not first or m >= PREP_BANKS:
                        pe.wait_ge(prep_copied, ITEMS1 * j + (m - PREP_BANKS + 1))
                    for c in range(IC):
                        turned = nc.tensor.transpose(prep_bank[m % PREP_BANKS][:, c * I:(c + 1) * I],
                                                     raw1[q % RAW][:, (m % 2) * IC + c, :], ident[:, :])
                    turned.then_inc(prep_made, 1)

            def squeeze_tile(j, t, between):
                s = SLOT1[t]
                pe.wait_ge(x_loaded[s], 16 * SLOT1.count(s) * j + 16 * (t // SLOTS + 1))
                for g in range(GROUPS):
                    if t == 0:
                        pe.wait_ge(prep_copied, ITEMS1 * j + 2 * (g + 1))
                    pe.wait_ge(group_taken, group1(j, t, g))
                    bank = mm_bank[g % MM_BANKS]
                    for c in range(GC):
                        mm = nc.tensor.matmul(bank[:, c * B1:(c + 1) * B1], w1t[:, g * GC + c, :],
                                              xt[s][:, :, g * GC + c], start=True, stop=True)
                    mm.then_inc(group_made, 1)
                    between(g)

            def nothing(g):
                pass

            for q in range(GROUPS):
                prep_w1(0, q, first=True)

            pe.wait_ge(bn2_worked, 1)
            for k in range(CHUNKS2):
                last = nc.tensor.transpose(mm_bank[1][:, k * PAIRS:(k + 1) * PAIRS],
                                           scale2[0:PAIRS, k * P:(k + 1) * P], ident[0:PAIRS, 0:PAIRS])
            last.then_inc(bn_turned, 1)

            with pe.Fori(0, CHUNKS1 - 1) as j:
                for t in range(LAST):
                    squeeze_tile(j, t, nothing)
                for q in range(RAW):
                    prep_w1(j + 1, q)

                def next_lot(g):
                    if 1 <= g <= GROUPS - RAW:
                        prep_w1(j + 1, g + 1)
                squeeze_tile(j, LAST, next_lot)

            def prep_w2(k, g):
                if g % 2 == 0:
                    pe.wait_ge(raw_scaled, LOTS2 * k + (LOTS1 + g // 2 + 1))
                pe.wait_ge(prep_copied, GROUPS * k + (N_W1 + g - 1))
                for c in range(IC):
                    turned = nc.tensor.transpose(prep_bank[(2 * g) % PREP_BANKS][:, c * P:(c + 1) * P],
                                                 raw2[(g // 2) % RAW][:, (g % 2) * IC + c, :], ident[:, :])
                turned.then_inc(prep_made, 1)

            def spread_shifts(k, g, first=False):
                if not first or g >= 2:
                    pe.wait_ge(spread_copied, GROUPS * k + (g - 1))
                for c in range(IC):
                    pair = g * IC + c
                    mm = nc.tensor.matmul(prep_bank[(2 * g + 1) % PREP_BANKS][:, c * P:(c + 1) * P],
                                          ones_at[:, pair:pair + 1].to_broadcast([R2, P]),
                                          t2p[:, :, bass.ts(k, D2)], start=True, stop=True)
                mm.then_inc(spread_made, 1)

            def expand_tile(k, t, between):
                pe.wait_ge(relu_done, (GROUPS // 2) * (B2 // B1) * (t + 1))
                for g in range(GROUPS):
                    if t == 0:
                        pe.wait_ge(prep_copied, GROUPS * k + (N_W1 + g + 1))
                    pe.wait_ge(group_taken, group2(k, t, g))
                    bank = mm_bank[g % MM_BANKS]
                    for c in range(GC):
                        mm = nc.tensor.matmul(bank[:, c * D2:(c + 1) * D2],
                                              h[:, g * GC + c, t * B2:(t + 1) * B2],
                                              w2t[:, g * GC + c, :], start=True, stop=True)
                    mm.then_inc(group_made, 1)
                    between(g)

            for t in range(LAST):
                squeeze_tile(CHUNKS1 - 1, t, nothing)
            pe.wait_ge(prep_copied, N_W1)
            for g in range(2):
                prep_w2(0, g)
                spread_shifts(0, g, first=True)
            squeeze_tile(CHUNKS1 - 1, LAST, nothing)
            for g in range(2, GROUPS):
                prep_w2(0, g)
                spread_shifts(0, g, first=True)

            with pe.Fori(0, CHUNKS2 - 1) as k:
                for t in range(TILES2 - 1):
                    expand_tile(k, t, nothing)
                for g in range(2):
                    prep_w2(k + 1, g)
                    spread_shifts(k + 1, g)

                def next_items(g):
                    if g >= 2:
                        prep_w2(k + 1, g)
                        spread_shifts(k + 1, g)
                expand_tile(k, TILES2 - 1, next_items)
            for t in range(TILES2):
                expand_tile(CHUNKS2 - 1, t, nothing)

        @block.scalar
        def _(act):
            for k, p in enumerate((b1, g1, be1, m1, v1)):
                act.dma_start(prm1[k], p).then_inc(params_loaded[0], 16)
            for k, p in enumerate((b2, g2, be2, m2, v2)):
                for part in range(PARTS):
                    act.dma_start(prm2[k][part * PAIRS:(part + 1) * PAIRS],
                                  p.rearrange("(c two) d -> c (two d)", two=2)).then_inc(params_loaded[1], 16)
            for layer, wk in enumerate((wk1, wk2)):
                act.wait_ge(sqrt_asked, layer + 1)
                nc.scalar.activation(wk[1], wk[1], ACT.Sqrt).then_inc(sqrt_done, 1)

            def copy_w1(j, q):
                for m in (2 * q, 2 * q + 1):
                    act.wait_ge(prep_made, ITEMS1 * j + (m + 1))
                    nc.scalar.activation(wt[:, m * BANK:(m + 1) * BANK], prep_bank[m % PREP_BANKS][:, :],
                                         ACT.Copy).then_inc(prep_copied, 1)

            def copy_w2(k, g):
                act.wait_ge(prep_made, GROUPS * k + (N_W1 + g + 1))
                nc.scalar.activation(wt[:, g * BANK:(g + 1) * BANK], prep_bank[(2 * g) % PREP_BANKS][:, :],
                                     ACT.Copy).then_inc(prep_copied, 1)

            for q in range(GROUPS):
                copy_w1(0, q)
            with act.Fori(0, CHUNKS1 - 1) as j:
                for q in range(GROUPS):
                    act.wait_ge(group_made, group1(j, LAST, q))
                    copy_w1(j + 1, q)

            for t in range(TILES1):
                for g in range(0, GROUPS, 2):
                    act.wait_ge(group_taken, taken(group1(CHUNKS1 - 1, t, g + 1)))
                    part = h[:, g * GC:(g + 2) * GC, t * B1:(t + 1) * B1]
                    nc.scalar.activation(part, part, ACT.Relu).then_inc(relu_done, 1)
            act.wait_ge(group_made, N_G1)
            for g in range(GROUPS):
                copy_w2(0, g)

            def sigmoids(k, t, g):
                act.wait_ge(group_taken, taken(group2(k, t, g)))
                part = yt[SLOT2[t]][:, :, (g - 1) * GC:(g + 1) * GC]
                nc.scalar.activation(part, part, ACT.Sigmoid).then_inc(sigm_done, 1)

            with act.Fori(0, CHUNKS2 - 1) as k:
                for t in range(TILES2):
                    for g in range(GROUPS):
                        if t == TILES2 - 1:
                            act.wait_ge(group_made, group2(k, t, g))
                            copy_w2(k + 1, g)
                        if g % 2 == 1:
                            sigmoids(k, t, g)
            for t in range(TILES2):
                for g in range(1, GROUPS, 2):
                    sigmoids(CHUNKS2 - 1, t, g)

        @block.vector
        def _(dve):
            steps = [0]

            def step(instruction):
                steps[0] += 1
                instruction.then_inc(dve_step, 1)
                dve.wait_ge(dve_step, steps[0])

            def batch_norm(layer, prm, wk):
                b, g, be, m, v = prm
                scale, y, shift, w = wk
                step(nc.vector.tensor_scalar(v, v, EPS, None, ALU.add))
                nc.vector.reciprocal(y, v).then_inc(sqrt_asked, 1)
                dve.wait_ge(sqrt_done, layer + 1)
                step(nc.vector.tensor_tensor(w, y, y, ALU.mult))
                step(nc.vector.tensor_tensor(w, w, v, ALU.mult))
                step(nc.vector.tensor_scalar(w, w, -0.5, 1.5, ALU.mult, ALU.add))
                step(nc.vector.tensor_tensor(y, y, w, ALU.mult))
                step(nc.vector.tensor_tensor(scale, g, y, ALU.mult))
                step(nc.vector.tensor_tensor(w, b, m, ALU.subtract))
                step(nc.vector.tensor_tensor(w, w, scale, ALU.mult))

            dve.wait_ge(params_loaded[0], 16 * 5)
            batch_norm(0, prm1, wk1)
            nc.vector.tensor_tensor(shift1, wk1[3], prm1[2], ALU.add).then_inc(bn1_worked, 1)
            dve.wait_ge(bn_turned, 1)
            nc.vector.tensor_copy(s1t[:, :], mm_bank[0][:, 0:C]).then_inc(bn1_ready, 1)
            nc.vector.tensor_copy(t1t[:, :], mm_bank[0][:, C:2 * C]).then_inc(bn1_ready, 1)

            dve.wait_ge(params_loaded[1], 16 * 5 * PARTS)
            batch_norm(1, prm2, wk2)
            step(nc.vector.tensor_copy(scale2.rearrange("p (k two d) -> p two k d", k=CHUNKS2, two=2),
                                       wk2[0].rearrange("p (two k d) -> p two k d", k=CHUNKS2, two=2)))
            rest = wk2[2]
            step(nc.vector.tensor_tensor(rest, wk2[3], prm2[2], ALU.add))
            for part in range(PARTS):
                rows = slice(part * PAIRS, (part + 1) * PAIRS)
                step(nc.vector.tensor_copy(part_bf, rest))
                step(nc.vector.tensor_copy(t2p[rows].rearrange("p two d -> p (two d)"), part_bf[rows]))
                if part < PARTS - 1:
                    step(nc.vector.tensor_tensor(rest, rest, part_bf, ALU.subtract))
            dve.wait_ge(ident_made, 2)
            for part in range(PARTS):
                rows = slice(part * PAIRS, (part + 1) * PAIRS)
                last = nc.vector.tensor_copy(ones_at[rows], ident[rows, rows])
            last.then_inc(bn2_worked, 1)
            dve.wait_ge(bn_turned, 2)
            nc.vector.tensor_copy(s2t[:, :, :].rearrange("p k c -> p (k c)"),
                                  mm_bank[1][:, 0:CHUNKS2 * PAIRS]).then_inc(bn2_ready, 1)
            dve.wait_ge(bn2_ready, 1)
            dve.sem_inc(group_taken, MM_BANKS)

            def add_group(j, t, g, base):
                dve.wait_ge(group_made, group1(j, t, g))
                nc.vector.tensor_tensor(h[:, g * GC:(g + 1) * GC, t * B1:(t + 1) * B1],
                                        mm_bank[g % MM_BANKS][:, :].rearrange("p (c b) -> p c b", b=B1),
                                        base, ALU.add).then_inc(group_taken, 1)

            dve.wait_ge(bn1_ready, 2)
            for t in range(TILES1):
                for g in range(GROUPS):
                    add_group(0, t, g, t1t[:, g * GC:(g + 1) * GC].unsqueeze(2).to_broadcast([P, GC, B1]))
            with dve.Fori(1, CHUNKS1) as j:
                for t in range(TILES1):
                    for g in range(GROUPS):
                        add_group(j, t, g, h[:, g * GC:(g + 1) * GC, t * B1:(t + 1) * B1])

            def copy_shifts(k, g):
                dve.wait_ge(spread_made, GROUPS * k + (g + 1))
                nc.vector.tensor_copy(shifts[:, g, :, :],
                                      prep_bank[(2 * g + 1) % PREP_BANKS][:, :].rearrange("p (c d) -> p d c", c=GC)
                                      ).then_inc(spread_copied, 1)

            dve.wait_ge(group_made, N_G1)
            for g in range(GROUPS):
                copy_shifts(0, g)

            def expand_out(k, first, last):
                for t in range(TILES2):
                    s = SLOT2[t]
                    if not first or s in SLOT2[:t]:
                        dve.wait_ge(stored[s], 16 * SLOT2.count(s) * k + 16 * SLOT2[:t].count(s))
                    for g in range(GROUPS):
                        if t == 0:
                            dve.wait_ge(spread_copied, GROUPS * k + (g + 1))
                        dve.wait_ge(group_made, group2(k, t, g))
                        nc.vector.tensor_tensor(yt[s][:, :, g * GC:(g + 1) * GC],
                                                mm_bank[g % MM_BANKS][:, :].rearrange("p (c d) -> p d c", c=GC),
                                                shifts[:, g, :, :], ALU.add).then_inc(group_taken, 1)
                        if t == TILES2 - 1 and not last and g >= 1:
                            dve.wait_ge(group_taken, taken(group2(k, t, g - 1)))
                            copy_shifts(k + 1, g - 1)
                if not last:
                    dve.wait_ge(group_taken, taken(group2(k, TILES2 - 1, GROUPS - 1)))
                    copy_shifts(k + 1, GROUPS - 1)

            expand_out(0, True, False)
            with dve.Fori(1, CHUNKS2 - 1) as k:
                expand_out(k, False, False)
            expand_out(CHUNKS2 - 1, False, True)


_INS = ["r_x", "L0_rec_W1", "L0_rec_b1", "L0_rec_g1", "L0_rec_be1", "L0_rec_m1", "L0_rec_v1",
        "L0_rec_W2", "L0_rec_b2", "L0_rec_g2", "L0_rec_be2", "L0_rec_m2", "L0_rec_v2"]


def kernel(**inputs):
    import numpy as _np
    import concourse.bacc as _bacc
    from concourse import mybir as _mybir
    from concourse.bass_utils import run_bass_kernel_spmd as _run

    nc = _bacc.Bacc("TRN2", target_bir_lowering=False, num_devices=1, dynamic_dma_scratch_size=1024)
    arrays, args = {}, []
    for name in _INS:
        a = _np.ascontiguousarray(inputs[name])
        arrays[name] = a
        args.append(nc.dram_tensor(name, a.shape, _mybir.dt.from_np(a.dtype), kind="ExternalInput").ap())
    shape = inputs["r_x"].shape
    args.append(nc.dram_tensor("out", shape, _mybir.dt.float32, kind="ExternalOutput").ap())
    squeeze_expand_gate_kernel(nc, *args)
    return _run(nc, [arrays], core_ids=[0]).results[0]["out"]
```

```python
import concourse.bass as bass
from concourse import mybir
from contextlib import ExitStack


def squeeze_expand_gate_kernel(nc, x, W1, b1, g1, be1, m1, v1, W2, b2, g2, be2, m2, v2, out):
    fp32, bf16 = mybir.dt.float32, mybir.dt.bfloat16
    ALU = mybir.AluOpType
    ACT = mybir.ActivationFunctionType
    P = nc.NUM_PARTITIONS
    EPS = 1e-5

    B, D, C = x.shape
    I = W1.shape[1]
    assert I == P and D % P == 0

    HALVES = 2
    TILES = B // (HALVES * P)
    CHUNKS = D // P
    BANK = 512
    GC = BANK // P
    GROUPS = C // GC
    LAST_T, LAST_J, LAST_G = TILES - 1, CHUNKS - 1, GROUPS - 1
    assert TILES == 2

    LOT = 2
    LOTS = GROUPS // LOT
    RAW = 4
    PIECES = 4
    STORES = 2
    PAIRS = C // 2
    PARTS = 3
    MM_BANKS = 4

    N_PHASE = CHUNKS * TILES * GROUPS
    N_ITEMS = CHUNKS * GROUPS

    with ExitStack() as ctx:
        def sb(name, shape, dt=fp32):
            return ctx.enter_context(nc.sbuf_tensor(name, shape, dt))

        def sem(name):
            return ctx.enter_context(nc.semaphore(name))

        h = sb("h", [P, C, TILES * P])
        wt = sb("wt", [P, C * P])
        wt_c = wt[:, :].rearrange("p (c n) -> p c n", c=C)
        spread = sb("spread", [P, C * P])
        shifts = spread[:, :].rearrange("p (g d c) -> p g d c", g=GROUPS, c=GC)
        slots = [sb(f"slot{t}", [P, P, C]) for t in range(TILES)]
        turned = [sb(f"turned{s}", [P, GC, P]) for s in range(2)]
        raw = [sb(f"raw{s}", [P, LOT * GC, P]) for s in range(RAW)]
        ident = sb("ident", [P, P])
        ones_at = sb("ones_at", [PARTS * PAIRS, PAIRS], bf16)
        s1t = sb("s1t", [P, C])
        t1t = sb("t1t", [P, C])
        s2t = sb("s2t", [P, CHUNKS, PAIRS, 2])
        t2p = sb("t2p", [PARTS * PAIRS, 2, D], bf16)

        R1, R2 = C, PARTS * PAIRS
        E2 = 2 * D
        tmp1 = h[:, C - 4:C, :].rearrange("p c b -> p (c b)")
        assert 7 * I <= 4 * TILES * P and 7 * E2 + E2 // 2 <= C * P
        prm1 = [tmp1[0:R1, k * I:(k + 1) * I] for k in range(7)]
        prm2 = [spread[0:R2, k * E2:(k + 1) * E2] for k in range(7)]
        part_bf = spread[0:R2, 7 * E2:7 * E2 + E2 // 2].bitcast(bf16)

        scale1, shift1, scale2 = prm1[1], prm1[0], prm2[1]

        psum = [ctx.enter_context(nc.psum_tensor(f"bank{k}", [P, BANK], fp32)) for k in range(8)]
        mm_bank = psum[0:MM_BANKS]
        turn_bank = psum[4:6]
        prep_bank1, spread_bank1 = [psum[6]], [psum[7]]
        prep_bank2, spread_bank2 = [psum[6], psum[4]], [psum[7], psum[5]]

        ident_made = sem("ident_made")
        params_loaded = [sem(f"params{k}_loaded") for k in (1, 2)]
        dve_step = sem("dve_step")
        root_asked = sem("root_asked")
        root_done = sem("root_done")
        bn1_worked = sem("bn1_worked")
        bn2_worked = sem("bn2_worked")
        bn_turned = sem("bn_turned")
        bn1_ready = sem("bn1_ready")
        bn2_ready = sem("bn2_ready")
        x_loaded = [sem(f"x_loaded{t}") for t in range(TILES)]
        raw_loaded = [sem(f"raw_loaded{s}") for s in range(RAW)]
        raw_scaled = sem("raw_scaled")
        turn_made = sem("turn_made")
        turn_copied = sem("turn_copied")
        prep_made = sem("prep_made")
        prep_copied = sem("prep_copied")
        spread_made = sem("spread_made")
        spread_copied = sem("spread_copied")
        group_made = sem("group_made")
        group_taken = sem("group_taken")
        relu_done = sem("relu_done")
        sigm_done = sem("sigm_done")
        stored = [sem(f"stored{t}") for t in range(TILES)]

        def products(half, phase, j, t, g):
            return (TILES * GROUPS) * j + (N_PHASE * (2 * half + phase) + t * GROUPS + g + 1)

        def turns(half, j, t, g):
            return (TILES * GROUPS) * j + (N_PHASE * half + t * GROUPS + g + 1)

        def items(half, phase, j, g):
            return GROUPS * j + (N_ITEMS * (2 * half + phase) + g + 1)

        def lots(half, phase, j, q):
            return LOTS * j + (N_ITEMS // LOT * (2 * half + phase) + q + 1)

        def spreads(half, j, g):
            return GROUPS * j + (N_ITEMS * half + g + 1)

        block = ctx.enter_context(nc.Block())

        @block.sync
        def _(sp):
            def load_x(half, j, t, p):
                n = P // PIECES
                row = (half * TILES + t) * P
                sp.dma_start(slots[t][:, p * n:(p + 1) * n, :],
                             x[row:row + P, bass.ds(j * P + p * n, n), :]).then_inc(x_loaded[t], 16)

            def load_lot(half, phase, j, q):
                if type(j) is int and lots(half, phase, j, q) > RAW or type(j) is not int:
                    sp.wait_ge(prep_made, items(half, phase, j, LOT * (q - RAW) + LOT - 1))
                c = slice(q * LOT * GC, (q + 1) * LOT * GC)
                src = (W1[c, :, bass.ts(j, P)].rearrange("c i d -> i c d") if phase == 0 else
                       W2[c, bass.ts(j, P), :].rearrange("c d i -> d c i"))
                sp.dma_start(raw[q % RAW][:, :, :], src).then_inc(raw_loaded[q % RAW], 16)

            for q in range(RAW):
                load_lot(0, 0, 0, q)
            for p in range(PIECES):
                load_x(0, 0, 0, p)
                load_lot(0, 0, 0, RAW + p)
            for p in range(PIECES):
                load_x(0, 0, LAST_T, p)

            for half in range(HALVES):
                with sp.Fori(0, LAST_J) as j:
                    for q in range(RAW):
                        load_lot(half, 0, j + 1, q)
                    sp.wait_ge(turn_made, turns(half, j, 0, LAST_G))
                    for p in range(PIECES):
                        load_x(half, j + 1, 0, p)
                        load_lot(half, 0, j + 1, RAW + p)
                    sp.wait_ge(turn_made, turns(half, j, LAST_T, LAST_G))
                    for p in range(PIECES):
                        load_x(half, j + 1, LAST_T, p)
                with sp.Fori(0, CHUNKS) as k:
                    for q in range(LOTS):
                        load_lot(half, 1, k, q)
                if half < HALVES - 1:
                    for q in range(LOTS):
                        load_lot(half + 1, 0, 0, q)
                    for t in range(TILES):
                        sp.wait_ge(stored[t], 16 * STORES * CHUNKS * (half + 1))
                        for p in range(PIECES):
                            load_x(half + 1, 0, t, p)

        @block.gpsimd
        def _(pool):
            nc.gpsimd.memset(ident[:, :], 0.0).then_inc(ident_made, 1)
            pool.wait_ge(ident_made, 1)
            nc.gpsimd.affine_select(out=ident[:, :], in_=ident[:, :], compare_op=ALU.not_equal, fill=1.0,
                                    base=0, pattern=[[-1, P]], channel_multiplier=1).then_inc(ident_made, 1)

            def scale_lot(half, phase, j, q, scales):
                use = (LOTS // RAW) * (CHUNKS * (2 * half + phase)) + q // RAW + 1
                pool.wait_ge(raw_loaded[q % RAW], (16 * LOTS // RAW) * j + 16 * use)
                r = raw[q % RAW][:, :, :]
                nc.gpsimd.tensor_tensor(r, r, scales.unsqueeze(2).to_broadcast([P, LOT * GC, P]),
                                        ALU.mult).then_inc(raw_scaled, 1)

            pool.wait_ge(bn1_ready, 1)
            for half in range(HALVES):
                with pool.Fori(0, CHUNKS) as j:
                    for q in range(LOTS):
                        scale_lot(half, 0, j, q, s1t[:, q * LOT * GC:(q + 1) * LOT * GC])
                if half == 0:
                    pool.wait_ge(bn2_ready, 1)
                for k in range(CHUNKS):
                    for q in range(LOTS):
                        scale_lot(half, 1, k, q, s2t[:, k, :, :].rearrange("p c two -> p (c two)")
                                  [:, q * LOT * GC:(q + 1) * LOT * GC])

        @block.tensor
        def _(pe):
            def turn(half, j, t, g):
                if g == 0:
                    tiles = 16 * PIECES * (CHUNKS * half + 1)
                    pe.wait_ge(x_loaded[t], (16 * PIECES) * j + tiles)
                for c in range(GC):
                    tr = nc.tensor.transpose(turn_bank[g % 2][:, c * P:(c + 1) * P],
                                             slots[t][:, :, g * GC + c], ident[:, :])
                tr.then_inc(turn_made, 1)

            def prep(half, phase, j, g, banks):
                if g % LOT == 0:
                    pe.wait_ge(raw_scaled, lots(half, phase, j, g // LOT))
                if type(j) is not int or items(half, phase, j, g) > len(banks):
                    pe.wait_ge(prep_copied, items(half, phase, j, g - len(banks)))
                for c in range(GC):
                    tr = nc.tensor.transpose(banks[g % len(banks)][:, c * P:(c + 1) * P],
                                             raw[g // LOT % RAW][:, g % LOT * GC + c, :], ident[:, :])
                tr.then_inc(prep_made, 1)

            def spread_shifts(half, k, g, banks):
                if type(k) is not int or spreads(half, k, g) > len(banks):
                    pe.wait_ge(spread_copied, spreads(half, k, g - len(banks)))
                for n in range(GC // 2):
                    pair = g * GC // 2 + n
                    mm = nc.tensor.matmul(banks[g % len(banks)][:, n * 2 * P:(n + 1) * 2 * P],
                                          ones_at[:, pair:pair + 1].to_broadcast([R2, P]),
                                          t2p[:, :, bass.ts(k, P)], start=True, stop=True)
                mm.then_inc(spread_made, 1)

            def squeeze_tile(half, j, t, turn_next, between):
                for g in range(GROUPS):
                    if g < LAST_G:
                        turn(half, j, t, g + 1)
                    else:
                        turn_next()
                    pe.wait_ge(turn_copied, turns(half, j, t, g))
                    if t == 0:
                        pe.wait_ge(prep_copied, items(half, 0, j, g))
                    pe.wait_ge(group_taken, products(half, 0, j, t, g))
                    for c in range(GC):
                        mm = nc.tensor.matmul(mm_bank[g % MM_BANKS][:, c * P:(c + 1) * P],
                                              wt_c[:, g * GC + c, :], turned[g % 2][:, c, :],
                                              start=True, stop=True)
                    mm.then_inc(group_made, 1)
                    between(g)

            def expand_tile(half, k, t, between):
                pe.wait_ge(relu_done, GROUPS // 2 * (TILES * half + t + 1))
                for g in range(GROUPS):
                    if t == 0:
                        pe.wait_ge(prep_copied, items(half, 1, k, g))
                    pe.wait_ge(group_taken, products(half, 1, k, t, g))
                    for c in range(GC):
                        mm = nc.tensor.matmul(mm_bank[g % MM_BANKS][:, c * P:(c + 1) * P],
                                              h[:, g * GC + c, t * P:(t + 1) * P], wt_c[:, g * GC + c, :],
                                              start=True, stop=True)
                    mm.then_inc(group_made, 1)
                    between(g)

            def nothing(g=0):
                pass

            pe.wait_ge(ident_made, 2)
            pe.wait_ge(bn1_worked, 1)
            nc.tensor.transpose(mm_bank[0][:, 0:C], scale1, ident[0:R1, 0:R1])
            nc.tensor.transpose(mm_bank[0][:, C:2 * C], shift1, ident[0:R1, 0:R1]).then_inc(bn_turned, 1)
            for g in range(GROUPS):
                prep(0, 0, 0, g, prep_bank2)

            for half in range(HALVES):
                pe.wait_ge(prep_copied, items(half, 0, 0, LAST_G))
                if half > 0:
                    pe.wait_ge(spread_copied, spreads(half - 1, LAST_J, LAST_G))
                turn(half, 0, 0, 0)
                with pe.Fori(0, LAST_J) as j:
                    squeeze_tile(half, j, 0, lambda: turn(half, j, LAST_T, 0), nothing)
                    squeeze_tile(half, j, LAST_T, lambda: turn(half, j + 1, 0, 0),
                                 lambda g: prep(half, 0, j + 1, g, prep_bank1))

                if half == 0:
                    pe.wait_ge(bn2_worked, 1)
                    pe.wait_ge(group_taken, products(0, 0, LAST_J, 0, MM_BANKS - 1))
                    for k in range(CHUNKS):
                        for two in range(2):
                            n = 2 * k + two
                            tr = nc.tensor.transpose(mm_bank[MM_BANKS - 1][:, n * PAIRS:(n + 1) * PAIRS],
                                                     scale2[0:PAIRS, two * D + k * P:two * D + (k + 1) * P],
                                                     ident[0:PAIRS, 0:PAIRS])
                    tr.then_inc(bn_turned, 1)
                    pe.wait_ge(bn2_ready, 1)

                squeeze_tile(half, LAST_J, 0, lambda: turn(half, LAST_J, LAST_T, 0), nothing)

                def first_of_phase2(g):
                    prep(half, 1, 0, g, prep_bank1)
                    spread_shifts(half, 0, g, spread_bank1)
                squeeze_tile(half, LAST_J, LAST_T, nothing, first_of_phase2)

                pe.wait_ge(prep_copied, items(half, 1, 0, LAST_G))
                pe.wait_ge(spread_copied, spreads(half, 0, LAST_G))
                with pe.Fori(0, LAST_J) as k:
                    expand_tile(half, k, 0, nothing)

                    def next_of_phase2(g):
                        prep(half, 1, k + 1, g, prep_bank2)
                        spread_shifts(half, k + 1, g, spread_bank2)
                    expand_tile(half, k, LAST_T, next_of_phase2)
                expand_tile(half, LAST_J, 0, nothing)
                expand_tile(half, LAST_J, LAST_T, nothing if half == HALVES - 1 else
                            lambda g: prep(half + 1, 0, 0, g, prep_bank2))

        @block.scalar
        def _(act):
            for k, p in enumerate((b1, g1, be1, m1, v1)):
                act.dma_start(prm1[k], p).then_inc(params_loaded[0], 16)
            for k, p in enumerate((b2, g2, be2, m2, v2)):
                for part in range(PARTS):
                    act.dma_start(prm2[k][part * PAIRS:(part + 1) * PAIRS],
                                  p.rearrange("(c two) d -> c (two d)", two=2)).then_inc(params_loaded[1], 16)

            def root(layer, y):
                act.wait_ge(root_asked, layer)
                nc.scalar.activation(y, y, ACT.Sqrt).then_inc(root_done, 1)

            root(1, prm1[5])

            def copy_turned(half, j, t, g):
                act.wait_ge(turn_made, turns(half, j, t, g))
                nc.scalar.activation(turned[g % 2][:, :, :].rearrange("p c b -> p (c b)"),
                                     turn_bank[g % 2][:, :], ACT.Copy).then_inc(turn_copied, 1)

            def copy_prep(half, phase, j, g, banks):
                act.wait_ge(prep_made, items(half, phase, j, g))
                nc.scalar.activation(wt[:, g * BANK:(g + 1) * BANK], banks[g % len(banks)][:, :],
                                     ACT.Copy).then_inc(prep_copied, 1)

            def relu(half, t, g):
                act.wait_ge(group_taken, products(half, 0, LAST_J, t, g) + MM_BANKS)
                part = h[:, (g - 1) * GC:(g + 1) * GC, t * P:(t + 1) * P]
                nc.scalar.activation(part, part, ACT.Relu).then_inc(relu_done, 1)

            def sigmoid(half, k, t, g):
                act.wait_ge(group_taken, products(half, 1, k, t, g) + MM_BANKS)
                part = slots[t][:, :, (g - 1) * GC:(g + 1) * GC]
                nc.scalar.activation(part, part, ACT.Sigmoid).then_inc(sigm_done, 1)

            def turned_tile(half, j, t, turned_next, between):
                for g in range(GROUPS):
                    if g < LAST_G:
                        copy_turned(half, j, t, g + 1)
                    else:
                        turned_next()
                    between(g)

            def output_tile(half, k, t, between):
                for g in range(GROUPS):
                    between(g)
                    if g % 2 == 1 and g > 2:
                        sigmoid(half, k, t, g - 2)
                sigmoid(half, k, t, LAST_G)
                act.wait_ge(sigm_done, (GROUPS // 2 * TILES) * k + GROUPS // 2 * (TILES * CHUNKS * half + t + 1))
                n = P // STORES
                row = (half * TILES + t) * P
                for p in range(STORES):
                    act.dma_start(out[row:row + P, bass.ds(k * P + p * n, n), :],
                                  slots[t][:, p * n:(p + 1) * n, :]).then_inc(stored[t], 16)

            def nothing(g=0):
                pass

            for g in range(GROUPS):
                copy_prep(0, 0, 0, g, prep_bank2)
            for half in range(HALVES):
                def turned_chunk(j, with_root2=False):
                    turned_tile(half, j, 0, lambda: copy_turned(half, j, LAST_T, 0), nothing)

                    def next_of_phase1(g):
                        act.wait_ge(group_made, products(half, 0, j, LAST_T, g))
                        copy_prep(half, 0, j + 1, g, prep_bank1)
                        if with_root2 and g == 5:
                            root(2, prm2[5])
                    turned_tile(half, j, LAST_T, lambda: copy_turned(half, j + 1, 0, 0), next_of_phase1)

                copy_turned(half, 0, 0, 0)
                turned_chunk(0, with_root2=half == 0)
                with act.Fori(1, LAST_J) as j:
                    turned_chunk(j)

                def relus(t, g):
                    if g % 2 == 1 and g > 2:
                        relu(half, t, g - 2)
                    if g == LAST_G:
                        relu(half, t, g)

                def first_of_phase2(g):
                    act.wait_ge(group_made, products(half, 0, LAST_J, LAST_T, g))
                    copy_prep(half, 1, 0, g, prep_bank1)
                    relus(LAST_T, g)
                turned_tile(half, LAST_J, 0, lambda: copy_turned(half, LAST_J, LAST_T, 0), lambda g: relus(0, g))
                turned_tile(half, LAST_J, LAST_T, nothing, first_of_phase2)

                def next_of_phase2(g):
                    act.wait_ge(group_made, products(half, 1, k, LAST_T, g))
                    copy_prep(half, 1, k + 1, g, prep_bank2)

                def next_half(g):
                    act.wait_ge(group_made, products(half, 1, LAST_J, LAST_T, g))
                    copy_prep(half + 1, 0, 0, g, prep_bank2)

                with act.Fori(0, LAST_J) as k:
                    output_tile(half, k, 0, nothing)
                    output_tile(half, k, LAST_T, next_of_phase2)
                output_tile(half, LAST_J, 0, nothing)
                output_tile(half, LAST_J, LAST_T, nothing if half == HALVES - 1 else next_half)
            for t in range(TILES):
                act.wait_ge(stored[t], 16 * STORES * CHUNKS * HALVES)

        @block.vector
        def _(dve):
            steps = [0]

            def step(instruction):
                steps[0] += 1
                instruction.then_inc(dve_step, 1)
                dve.wait_ge(dve_step, steps[0])

            def add_group(half, j, t, g, base):
                dve.wait_ge(group_made, products(half, 0, j, t, g))
                nc.vector.tensor_tensor(h[:, g * GC:(g + 1) * GC, t * P:(t + 1) * P],
                                        mm_bank[g % MM_BANKS][:, :].rearrange("p (c b) -> p c b", c=GC),
                                        base, ALU.add).then_inc(group_taken, 1)

            def so_far(t, g):
                return h[:, g * GC:(g + 1) * GC, t * P:(t + 1) * P]

            def shift1_of(g):
                return t1t[:, g * GC:(g + 1) * GC].unsqueeze(2).to_broadcast([P, GC, P])

            def copy_shifts(half, k, g, banks):
                dve.wait_ge(spread_made, spreads(half, k, g))
                nc.vector.tensor_copy(shifts[:, g, :, :],
                                      banks[g % len(banks)][:, :].rearrange("p (c d) -> p d c", c=GC)
                                      ).then_inc(spread_copied, 1)

            def output_tile(half, k, t, spread_next):
                if type(k) is int and k == 0:
                    dve.wait_ge(turn_made, turns(half, LAST_J, t, LAST_G))
                else:
                    dve.wait_ge(stored[t], (16 * STORES) * k + 16 * STORES * CHUNKS * half)
                for g in range(GROUPS):
                    if t == 0:
                        dve.wait_ge(spread_copied, spreads(half, k, g))
                    dve.wait_ge(group_made, products(half, 1, k, t, g))
                    nc.vector.tensor_tensor(slots[t][:, :, g * GC:(g + 1) * GC],
                                            mm_bank[g % MM_BANKS][:, :].rearrange("p (c d) -> p d c", c=GC),
                                            shifts[:, g, :, :], ALU.add).then_inc(group_taken, 1)
                    if spread_next and g > 0:
                        dve.wait_ge(group_taken, products(half, 1, k, t, g - 1) + MM_BANKS)
                        copy_shifts(half, k + 1, g - 1, spread_bank2)
                if spread_next:
                    dve.wait_ge(group_taken, products(half, 1, k, t, LAST_G) + MM_BANKS)
                    copy_shifts(half, k + 1, LAST_G, spread_bank2)

            b, g_, be, m, v, y, w = prm1
            dve.wait_ge(params_loaded[0], 16 * 5)
            step(nc.vector.tensor_scalar(v, v, EPS, None, ALU.add))
            nc.vector.reciprocal(y, v).then_inc(root_asked, 1)
            dve.wait_ge(root_done, 1)
            step(nc.vector.tensor_tensor(w, y, y, ALU.mult))
            step(nc.vector.tensor_tensor(w, w, v, ALU.mult))
            step(nc.vector.tensor_scalar(w, w, -0.5, 1.5, ALU.mult, ALU.add))
            step(nc.vector.tensor_tensor(y, y, w, ALU.mult))
            step(nc.vector.tensor_tensor(g_, g_, y, ALU.mult))
            step(nc.vector.tensor_tensor(b, b, m, ALU.subtract))
            step(nc.vector.tensor_tensor(b, b, g_, ALU.mult))
            nc.vector.tensor_tensor(b, b, be, ALU.add).then_inc(bn1_worked, 1)
            dve.wait_ge(bn_turned, 1)
            nc.vector.tensor_copy(s1t[:, :], mm_bank[0][:, 0:C]).then_inc(bn1_ready, 1)
            nc.vector.tensor_copy(t1t[:, :], mm_bank[0][:, C:2 * C]).then_inc(bn1_ready, 1)
            dve.wait_ge(bn1_ready, 2)
            dve.sem_inc(group_taken, MM_BANKS)

            def layer2_step(n):
                b, g_, be, m, v, y, w = prm2
                quarter = E2 // 4
                if n == 0:
                    dve.wait_ge(params_loaded[1], 16 * 5 * PARTS)
                    step(nc.vector.tensor_scalar(v, v, EPS, None, ALU.add))
                if n < 4:
                    inv = nc.vector.reciprocal(y[:, n * quarter:(n + 1) * quarter], v[:, n * quarter:(n + 1) * quarter])
                    if n == 3:
                        inv.then_inc(root_asked, 1)
                elif n == 4:
                    dve.wait_ge(root_done, 2)
                    step(nc.vector.tensor_tensor(w, y, y, ALU.mult))
                elif n == 5:
                    step(nc.vector.tensor_tensor(w, w, v, ALU.mult))
                elif n == 6:
                    step(nc.vector.tensor_scalar(w, w, -0.5, 1.5, ALU.mult, ALU.add))
                elif n == 7:
                    step(nc.vector.tensor_tensor(y, y, w, ALU.mult))
                elif n == 8:
                    step(nc.vector.tensor_tensor(g_, g_, y, ALU.mult))
                elif n == 9:
                    step(nc.vector.tensor_tensor(b, b, m, ALU.subtract))
                elif n == 10:
                    step(nc.vector.tensor_tensor(b, b, g_, ALU.mult))
                elif n == 11:
                    step(nc.vector.tensor_tensor(b, b, be, ALU.add))
                elif n - 12 < PARTS:
                    rows = slice((n - 12) * PAIRS, (n - 11) * PAIRS)
                    step(nc.vector.tensor_copy(part_bf, b))
                    step(nc.vector.tensor_copy(t2p[rows].rearrange("p two d -> p (two d)"), part_bf[rows]))
                    step(nc.vector.tensor_tensor(b, b, part_bf, ALU.subtract))
                else:
                    dve.wait_ge(ident_made, 2)
                    for part in range(PARTS):
                        rows = slice(part * PAIRS, (part + 1) * PAIRS)
                        last = nc.vector.tensor_copy(ones_at[rows], ident[rows, rows])
                    last.then_inc(bn2_worked, 1)

            assert GROUPS >= 13 + PARTS
            for half in range(HALVES):
                for t in range(TILES):
                    for g in range(GROUPS):
                        add_group(half, 0, t, g, shift1_of(g))
                        if half == 0 and t == LAST_T:
                            layer2_step(g)
                with dve.Fori(1, LAST_J) as j:
                    for t in range(TILES):
                        for g in range(GROUPS):
                            add_group(half, j, t, g, so_far(t, g))
                if half == 0:
                    dve.wait_ge(bn_turned, 2)
                    nc.vector.tensor_copy(s2t[:, :, :, :].rearrange("p k c two -> p k two c"),
                                          mm_bank[MM_BANKS - 1][:, 0:CHUNKS * C].rearrange(
                                              "p (k two c) -> p k two c", k=CHUNKS, two=2)
                                          ).then_inc(bn2_ready, 1)
                else:
                    dve.wait_ge(group_taken, products(half - 1, 1, LAST_J, LAST_T, LAST_G) + MM_BANKS)
                for t in range(TILES):
                    for g in range(GROUPS):
                        add_group(half, LAST_J, t, g, so_far(t, g))
                        if t == LAST_T:
                            copy_shifts(half, 0, g, spread_bank1)

                for t in range(TILES):
                    output_tile(half, 0, t, t == LAST_T)
                with dve.Fori(1, LAST_J) as k:
                    for t in range(TILES):
                        output_tile(half, k, t, t == LAST_T)
                for t in range(TILES):
                    output_tile(half, LAST_J, t, False)


_INS = ["r_x", "L0_rec_W1", "L0_rec_b1", "L0_rec_g1", "L0_rec_be1", "L0_rec_m1", "L0_rec_v1",
        "L0_rec_W2", "L0_rec_b2", "L0_rec_g2", "L0_rec_be2", "L0_rec_m2", "L0_rec_v2"]


def kernel(**inputs):
    import numpy as _np
    import concourse.bacc as _bacc
    from concourse import mybir as _mybir
    from concourse.bass_utils import run_bass_kernel_spmd as _run

    nc = _bacc.Bacc("TRN2", target_bir_lowering=False, num_devices=1, dynamic_dma_scratch_size=1024)
    arrays, args = {}, []
    for name in _INS:
        a = _np.ascontiguousarray(inputs[name])
        arrays[name] = a
        args.append(nc.dram_tensor(name, a.shape, _mybir.dt.from_np(a.dtype), kind="ExternalInput").ap())
    shape = inputs["r_x"].shape
    args.append(nc.dram_tensor("out", shape, _mybir.dt.float32, kind="ExternalOutput").ap())
    squeeze_expand_gate_kernel(nc, *args)
    return _run(nc, [arrays], core_ids=[0]).results[0]["out"]
```

```python
import concourse.bass as bass
from concourse import mybir
from contextlib import ExitStack


def squeeze_expand_gate_kernel(nc, x, W1, b1, g1, be1, m1, v1, W2, b2, g2, be2, m2, v2, out):
    fp32, bf16 = mybir.dt.float32, mybir.dt.bfloat16
    ALU = mybir.AluOpType
    ACT = mybir.ActivationFunctionType
    P = nc.NUM_PARTITIONS
    EPS = 1e-5

    B, D, C = x.shape
    I = W1.shape[1]
    assert I == P and D % P == 0

    HALVES = 2
    TILES = B // (HALVES * P)
    CHUNKS = D // P
    BANK = 512
    GC = BANK // P
    GROUPS = C // GC
    LAST_T, LAST_J, LAST_G = TILES - 1, CHUNKS - 1, GROUPS - 1
    assert TILES == 2

    LOT = 2
    LOTS = GROUPS // LOT
    RAW = 4
    PIECES = 4
    LEAD = (LOT, RAW * LOT)
    AHEAD = 2
    PAIRS = C // 2
    PARTS = 3
    MM_BANKS = 4

    N_PHASE = CHUNKS * TILES * GROUPS
    N_ITEMS = CHUNKS * GROUPS

    with ExitStack() as ctx:
        def sb(name, shape, dt=fp32):
            return ctx.enter_context(nc.sbuf_tensor(name, shape, dt))

        def sem(name):
            return ctx.enter_context(nc.semaphore(name))

        h = sb("h", [P, C, TILES * P])
        wt = sb("wt", [P, C * P])
        wt_c = wt[:, :].rearrange("p (c n) -> p c n", c=C)
        spread = sb("spread", [P, P * C])
        shifts = spread[:, :].rearrange("p (d c) -> p d c", c=C)
        slots = [sb(f"slot{s}", [P, P, C]) for s in range(TILES)]
        turned = [sb(f"turned{s}", [P, GC, P]) for s in range(2)]
        raw = [sb(f"raw{s}", [P, LOT * GC, P]) for s in range(RAW)]
        ident = sb("ident", [P, P])
        ones_at = sb("ones_at", [PARTS * PAIRS, PAIRS], bf16)
        s1t = sb("s1t", [P, C])
        t1t = sb("t1t", [P, C])
        s2t = sb("s2t", [P, CHUNKS, PAIRS, 2])
        t2p = sb("t2p", [PARTS * PAIRS, 2, D], bf16)

        R1, R2 = C, PARTS * PAIRS
        E2 = 2 * P
        tmp1 = h[:, C - 4:C, :].rearrange("p c b -> p (c b)")
        assert CHUNKS * PAIRS == P and 7 * I <= 4 * TILES * P
        prm1 = [tmp1[0:R1, k * I:(k + 1) * I] for k in range(7)]
        prm2 = [spread[:, k * E2:(k + 1) * E2] for k in range(7)]
        part_bf = [spread[:, k * E2:k * E2 + E2 // 2].bitcast(bf16) for k in range(7, 7 + PARTS)]

        scale1, shift1, scale2 = prm1[1], prm1[0], prm2[1]

        psum = [ctx.enter_context(nc.psum_tensor(f"bank{k}", [P, BANK], fp32)) for k in range(8)]
        mm_bank = psum[0:MM_BANKS]
        turn_bank = psum[4:6]
        prep_bank1, spread_bank1 = [psum[6]], [psum[7]]
        prep_bank2, spread_bank2 = [psum[6], psum[4]], [psum[7], psum[5]]
        prep_bank0 = [psum[6], psum[7]]
        scale2_bank = psum[7]

        ident_made = sem("ident_made")
        params_loaded = [sem(f"params{k}_loaded") for k in (1, 2)]
        dve_step = sem("dve_step")
        root_asked = sem("root_asked")
        root_done = sem("root_done")
        bn1_worked = sem("bn1_worked")
        bn2_worked = sem("bn2_worked")
        bn_turned = sem("bn_turned")
        bn1_ready = sem("bn1_ready")
        bn2_ready = sem("bn2_ready")
        x_loaded = [sem(f"x_loaded{t}") for t in range(TILES)]
        raw_loaded = [sem(f"raw_loaded{s}") for s in range(RAW)]
        raw_scaled = sem("raw_scaled")
        turn_made = sem("turn_made")
        turn_copied = sem("turn_copied")
        prep_made = sem("prep_made")
        prep_copied = sem("prep_copied")
        spread_made = sem("spread_made")
        spread_copied = sem("spread_copied")
        group_made = sem("group_made")
        group_taken = sem("group_taken")
        relu_done = sem("relu_done")
        sigm_done = sem("sigm_done")
        stored = [[sem(f"stored{t}_{p}") for p in range(PIECES)] for t in range(TILES)]
        last_stored = [sem(f"last_stored{p}") for p in range(PIECES)]

        def x_tile(half, t):
            return slots[(t + half) % TILES]

        def out_tile(half, k, t):
            return shifts if type(k) is int and k == LAST_J and t == LAST_T else x_tile(half, t)

        def stores(half, k, t):
            return 16 * k + 16 * ((CHUNKS if t < LAST_T else LAST_J) * half + 1)

        def products(half, phase, j, t, g):
            return (TILES * GROUPS) * j + (N_PHASE * (2 * half + phase) + t * GROUPS + g + 1)

        def turns(half, j, t, g):
            return (TILES * GROUPS) * j + (N_PHASE * half + t * GROUPS + g + 1)

        def items(half, phase, j, g):
            return GROUPS * j + (N_ITEMS * (2 * half + phase) + g + 1)

        def lots(half, phase, j, q):
            return LOTS * j + (N_ITEMS // LOT * (2 * half + phase) + q + 1)

        def spreads(half, j, g):
            return GROUPS * j + (N_ITEMS * half + g + 1)

        layer1, layer2 = (b1, g1, be1, m1, v1), (b2, g2, be2, m2, v2)
        block = ctx.enter_context(nc.Block())

        @block.sync
        def _(sp):
            def load_x(half, j, t, p):
                n = P // PIECES
                row = (half * TILES + t) * P
                sp.dma_start(x_tile(half, t)[:, p * n:(p + 1) * n, :],
                             x[row:row + P, bass.ds(j * P + p * n, n), :]).then_inc(x_loaded[t], 16)

            def load_lot(half, phase, j, q):
                if type(j) is int and lots(half, phase, j, q) > RAW or type(j) is not int:
                    sp.wait_ge(prep_made, items(half, phase, j, LOT * (q - RAW) + LOT - 1))
                c = slice(q * LOT * GC, (q + 1) * LOT * GC)
                src = (W1[c, :, bass.ts(j, P)].rearrange("c i d -> i c d") if phase == 0 else
                       W2[c, bass.ts(j, P), :].rearrange("c d i -> d c i"))
                sp.dma_start(raw[q % RAW][:, :, :], src).then_inc(raw_loaded[q % RAW], 16)

            load_x(0, 0, 0, 0)
            for k in range(3, 5):
                sp.dma_start(prm1[k], layer1[k]).then_inc(params_loaded[0], 16)
            load_lot(0, 0, 0, 0)
            for p in range(1, PIECES):
                load_x(0, 0, 0, p)
            for q in range(1, LOTS - 2):
                load_lot(0, 0, 0, q)
            for p in range(PIECES):
                if p >= PIECES - 2:
                    load_lot(0, 0, 0, LOTS - PIECES + p)
                load_x(0, 0, LAST_T, p)
                for k in range(5):
                    sp.dma_start(prm2[k][p * PAIRS:(p + 1) * PAIRS].rearrange("c (two d) -> c two d", two=2),
                                 layer2[k][:, bass.ts(p, P)].rearrange("(c two) d -> c two d", two=2)
                                 ).then_inc(params_loaded[1], 16)
            assert PIECES == CHUNKS

            for half in range(HALVES):
                with sp.Fori(0, LAST_J) as j:
                    for q in range(RAW):
                        load_lot(half, 0, j + 1, q)
                    sp.wait_ge(turn_made, turns(half, j, 0, LAST_G))
                    for p in range(PIECES):
                        load_x(half, j + 1, 0, p)
                        load_lot(half, 0, j + 1, RAW + p)
                    sp.wait_ge(turn_made, turns(half, j, LAST_T, LAST_G))
                    for p in range(PIECES):
                        load_x(half, j + 1, LAST_T, p)
                with sp.Fori(0, CHUNKS) as k:
                    for q in range(LOTS):
                        load_lot(half, 1, k, q)
                if half < HALVES - 1:
                    for t in range(TILES):
                        for q in range(t * RAW, (t + 1) * RAW):
                            load_lot(half + 1, 0, 0, q)
                        for p in range(PIECES):
                            sp.wait_ge(stored[LAST_T - t][p], stores(half, LAST_J - 1 if t == 0 else LAST_J, LAST_T - t))
                            load_x(half + 1, 0, t, p)

        @block.gpsimd
        def _(pool):
            nc.gpsimd.memset(ident[:, :], 0.0).then_inc(ident_made, 1)
            pool.wait_ge(ident_made, 1)
            nc.gpsimd.affine_select(out=ident[:, :], in_=ident[:, :], compare_op=ALU.not_equal, fill=1.0,
                                    base=0, pattern=[[-1, P]], channel_multiplier=1).then_inc(ident_made, 1)

            def scale_lot(half, phase, j, q, scales):
                use = (LOTS // RAW) * (CHUNKS * (2 * half + phase)) + q // RAW + 1
                pool.wait_ge(raw_loaded[q % RAW], (16 * LOTS // RAW) * j + 16 * use)
                r = raw[q % RAW][:, :, :]
                nc.gpsimd.tensor_tensor(r, r, scales.unsqueeze(2).to_broadcast([P, LOT * GC, P]),
                                        ALU.mult).then_inc(raw_scaled, 1)

            pool.wait_ge(bn1_ready, 1)
            for half in range(HALVES):
                with pool.Fori(0, CHUNKS) as j:
                    for q in range(LOTS):
                        scale_lot(half, 0, j, q, s1t[:, q * LOT * GC:(q + 1) * LOT * GC])
                if half == 0:
                    pool.wait_ge(bn2_ready, 1)
                for k in range(CHUNKS):
                    for q in range(LOTS):
                        scale_lot(half, 1, k, q, s2t[:, k, :, :].rearrange("p c two -> p (c two)")
                                  [:, q * LOT * GC:(q + 1) * LOT * GC])

        @block.tensor
        def _(pe):
            def turn(half, j, t, g):
                if g == 0:
                    tiles = 16 * PIECES * (CHUNKS * half + 1)
                    pe.wait_ge(x_loaded[t], (16 * PIECES) * j + tiles)
                for c in range(GC):
                    tr = nc.tensor.transpose(turn_bank[g % 2][:, c * P:(c + 1) * P],
                                             x_tile(half, t)[:, :, g * GC + c], ident[:, :])
                tr.then_inc(turn_made, 1)

            def prep(half, phase, j, g, banks):
                if g % LOT == 0:
                    pe.wait_ge(raw_scaled, lots(half, phase, j, g // LOT))
                if type(j) is not int or items(half, phase, j, g) > len(banks):
                    pe.wait_ge(prep_copied, items(half, phase, j, g - len(banks)))
                for c in range(GC):
                    tr = nc.tensor.transpose(banks[g % len(banks)][:, c * P:(c + 1) * P],
                                             raw[g // LOT % RAW][:, g % LOT * GC + c, :], ident[:, :])
                tr.then_inc(prep_made, 1)

            def spread_shifts(half, k, g, banks):
                if type(k) is not int or spreads(half, k, g) > len(banks):
                    pe.wait_ge(spread_copied, spreads(half, k, g - len(banks)))
                for n in range(GC // 2):
                    pair = g * GC // 2 + n
                    mm = nc.tensor.matmul(banks[g % len(banks)][:, n * 2 * P:(n + 1) * 2 * P],
                                          ones_at[:, pair:pair + 1].to_broadcast([R2, P]),
                                          t2p[:, :, bass.ts(k, P)], start=True, stop=True)
                mm.then_inc(spread_made, 1)

            def squeeze_tile(half, j, t, turn_next, between):
                for g in range(GROUPS):
                    if g < LAST_G:
                        turn(half, j, t, g + 1)
                    else:
                        turn_next()
                    pe.wait_ge(turn_copied, turns(half, j, t, g))
                    if t == 0:
                        pe.wait_ge(prep_copied, items(half, 0, j, g))
                    pe.wait_ge(group_taken, products(half, 0, j, t, g))
                    for c in range(GC):
                        mm = nc.tensor.matmul(mm_bank[g % MM_BANKS][:, c * P:(c + 1) * P],
                                              wt_c[:, g * GC + c, :], turned[g % 2][:, c, :],
                                              start=True, stop=True)
                    mm.then_inc(group_made, 1)
                    between(g)

            def expand_tile(half, k, t, between):
                pe.wait_ge(relu_done, GROUPS // 2 * (TILES * half + t + 1))
                for g in range(GROUPS):
                    if t == 0:
                        pe.wait_ge(prep_copied, items(half, 1, k, g))
                    pe.wait_ge(group_taken, products(half, 1, k, t, g))
                    for c in range(GC):
                        mm = nc.tensor.matmul(mm_bank[g % MM_BANKS][:, c * P:(c + 1) * P],
                                              h[:, g * GC + c, t * P:(t + 1) * P], wt_c[:, g * GC + c, :],
                                              start=True, stop=True)
                    mm.then_inc(group_made, 1)
                    between(g)

            def nothing(g=0):
                pass

            pe.wait_ge(ident_made, 2)
            pe.wait_ge(bn1_worked, 1)
            nc.tensor.transpose(mm_bank[0][:, 0:C], scale1, ident[0:R1, 0:R1])
            nc.tensor.transpose(mm_bank[0][:, C:2 * C], shift1, ident[0:R1, 0:R1]).then_inc(bn_turned, 1)
            for g in range(LEAD[0]):
                prep(0, 0, 0, g, prep_bank0)

            for half in range(HALVES):
                def squeeze_chunk(j, rest_of_first):
                    squeeze_tile(half, j, 0, lambda: turn(half, j, LAST_T, 0), rest_of_first)
                    squeeze_tile(half, j, LAST_T, lambda: turn(half, j + 1, 0, 0),
                                 lambda g: prep(half, 0, j + 1, g, prep_bank1))

                def rest_of_first(g):
                    if LEAD[half] <= g + AHEAD < GROUPS:
                        prep(half, 0, 0, g + AHEAD, prep_bank0)

                if half == 0:
                    turn(half, 0, 0, 0)
                squeeze_chunk(0, rest_of_first)
                with pe.Fori(1, LAST_J) as j:
                    squeeze_chunk(j, nothing)

                if half == 0:
                    pe.wait_ge(bn2_worked, 1)
                    for two in range(2):
                        tr = nc.tensor.transpose(scale2_bank[:, two * P:(two + 1) * P],
                                                 scale2[:, two * P:(two + 1) * P], ident[:, :])
                    tr.then_inc(bn_turned, 1)

                squeeze_tile(half, LAST_J, 0, lambda: turn(half, LAST_J, LAST_T, 0), nothing)

                def first_of_phase2(g):
                    prep(half, 1, 0, g, prep_bank1)
                    if half == 0 and g == 0:
                        pe.wait_ge(bn2_ready, 1)
                    spread_shifts(half, 0, g, spread_bank1)
                squeeze_tile(half, LAST_J, LAST_T, nothing, first_of_phase2)

                with pe.Fori(0, LAST_J) as k:
                    expand_tile(half, k, 0, nothing)

                    def next_of_phase2(g):
                        if g == 0:
                            pe.wait_ge(spread_copied, spreads(half, k, LAST_G))
                        prep(half, 1, k + 1, g, prep_bank2)
                        spread_shifts(half, k + 1, g, spread_bank2)
                    expand_tile(half, k, LAST_T, next_of_phase2)
                expand_tile(half, LAST_J, 0, nothing)

                def first_of_next_half(g):
                    if half < HALVES - 1 and g < LEAD[half + 1]:
                        prep(half + 1, 0, 0, g, prep_bank2)
                    if half < HALVES - 1 and g == LAST_G - 1:
                        pe.wait_ge(prep_copied, items(half + 1, 0, 0, LEAD[half + 1] - 1))
                        pe.wait_ge(spread_copied, spreads(half, LAST_J, LAST_G))
                        turn(half + 1, 0, 0, 0)
                expand_tile(half, LAST_J, LAST_T, first_of_next_half)

        @block.scalar
        def _(act):
            for k in range(3):
                act.dma_start(prm1[k], layer1[k]).then_inc(params_loaded[0], 16)

            def root(layer, y):
                act.wait_ge(root_asked, layer)
                nc.scalar.activation(y, y, ACT.Sqrt).then_inc(root_done, 1)

            root(1, prm1[5])

            def copy_turned(half, j, t, g):
                act.wait_ge(turn_made, turns(half, j, t, g))
                nc.scalar.activation(turned[g % 2][:, :, :].rearrange("p c b -> p (c b)"),
                                     turn_bank[g % 2][:, :], ACT.Copy).then_inc(turn_copied, 1)

            def copy_prep(half, phase, j, g, banks):
                act.wait_ge(prep_made, items(half, phase, j, g))
                nc.scalar.activation(wt[:, g * BANK:(g + 1) * BANK], banks[g % len(banks)][:, :],
                                     ACT.Copy).then_inc(prep_copied, 1)

            def relu(half, t, g):
                act.wait_ge(group_taken, products(half, 0, LAST_J, t, g) + MM_BANKS)
                part = h[:, (g - 1) * GC:(g + 1) * GC, t * P:(t + 1) * P]
                nc.scalar.activation(part, part, ACT.Relu).then_inc(relu_done, 1)

            def sigmoid(half, k, t, g):
                act.wait_ge(group_taken, products(half, 1, k, t, g) + MM_BANKS)
                part = out_tile(half, k, t)[:, :, (g - 1) * GC:(g + 1) * GC]
                nc.scalar.activation(part, part, ACT.Sigmoid).then_inc(sigm_done, 1)

            def turned_tile(half, j, t, turned_next, between):
                for g in range(GROUPS):
                    if g < LAST_G:
                        copy_turned(half, j, t, g + 1)
                    else:
                        turned_next()
                    between(g)

            def output_tile(half, k, t, between):
                for g in range(GROUPS):
                    between(g)
                    if g % 2 == 1 and g > 2:
                        sigmoid(half, k, t, g - 2)
                sigmoid(half, k, t, LAST_G)
                act.wait_ge(sigm_done, (GROUPS // 2 * TILES) * k + GROUPS // 2 * (TILES * CHUNKS * half + t + 1))

            def store(half, k, t, p):
                n = P // PIECES
                row = (half * TILES + t) * P
                tile = out_tile(half, k, t)
                act.dma_start(out[row:row + P, bass.ds(k * P + p * n, n), :], tile[:, p * n:(p + 1) * n, :]
                              ).then_inc(last_stored[p] if tile is shifts else stored[t][p], 16)

            def output_chunk(half, k, between):
                output_tile(half, k, 0, nothing)
                store(half, k, 0, 0)

                def between_and_store(g):
                    between(g)
                    if g % 3 == 2 and g // 3 + 1 < PIECES:
                        store(half, k, 0, g // 3 + 1)
                output_tile(half, k, LAST_T, between_and_store)
                if out_tile(half, k, LAST_T) is not shifts or half == HALVES - 1:
                    for p in range(PIECES):
                        store(half, k, LAST_T, p)

            def nothing(g=0):
                pass

            for g in range(LEAD[0]):
                copy_prep(0, 0, 0, g, prep_bank0)
            for half in range(HALVES):
                def turned_chunk(j, rest_of_first, first=False):
                    turned_tile(half, j, 0, lambda: copy_turned(half, j, LAST_T, 0), rest_of_first)

                    def next_of_phase1(g):
                        act.wait_ge(group_made, products(half, 0, j, LAST_T, g))
                        copy_prep(half, 0, j + 1, g, prep_bank1)
                        if first and half == 0 and g == 3:
                            root(2, prm2[5])
                        if first and half > 0 and g >= GROUPS - 2 * PIECES and g % 2 == 1:
                            store(half - 1, LAST_J, LAST_T, (g - LAST_G) // 2 + PIECES - 1)
                    turned_tile(half, j, LAST_T, lambda: copy_turned(half, j + 1, 0, 0), next_of_phase1)

                def rest_of_first(g):
                    if LEAD[half] <= g + AHEAD < GROUPS:
                        copy_prep(half, 0, 0, g + AHEAD, prep_bank0)

                if half == 0:
                    copy_turned(half, 0, 0, 0)
                turned_chunk(0, rest_of_first, first=True)
                with act.Fori(1, LAST_J) as j:
                    turned_chunk(j, nothing)

                def relus(t, g):
                    if g % 2 == 1 and g > 2:
                        relu(half, t, g - 2)
                    if g == LAST_G:
                        relu(half, t, g)

                def first_of_phase2(g):
                    act.wait_ge(group_made, products(half, 0, LAST_J, LAST_T, g))
                    copy_prep(half, 1, 0, g, prep_bank1)
                    relus(LAST_T, g)
                turned_tile(half, LAST_J, 0, lambda: copy_turned(half, LAST_J, LAST_T, 0), lambda g: relus(0, g))
                turned_tile(half, LAST_J, LAST_T, nothing, first_of_phase2)

                def next_of_phase2(g):
                    act.wait_ge(group_made, products(half, 1, k, LAST_T, g))
                    copy_prep(half, 1, k + 1, g, prep_bank2)

                def first_of_next_half(g):
                    if half < HALVES - 1 and g < LEAD[half + 1]:
                        act.wait_ge(group_made, products(half, 1, LAST_J, LAST_T, g))
                        copy_prep(half + 1, 0, 0, g, prep_bank2)
                    if half < HALVES - 1 and g == LAST_G:
                        copy_turned(half + 1, 0, 0, 0)

                with act.Fori(0, LAST_J) as k:
                    output_chunk(half, k, next_of_phase2)
                output_chunk(half, LAST_J, first_of_next_half)
            for t in range(TILES):
                for p in range(PIECES):
                    act.wait_ge(stored[t][p], stores(HALVES - 1, LAST_J - t, t))
            for p in range(PIECES):
                act.wait_ge(last_stored[p], 16 * HALVES)

        @block.vector
        def _(dve):
            steps = [0]

            def step(instruction):
                steps[0] += 1
                instruction.then_inc(dve_step, 1)
                dve.wait_ge(dve_step, steps[0])

            def add_group(half, j, t, g, base):
                dve.wait_ge(group_made, products(half, 0, j, t, g))
                nc.vector.tensor_tensor(h[:, g * GC:(g + 1) * GC, t * P:(t + 1) * P],
                                        mm_bank[g % MM_BANKS][:, :].rearrange("p (c b) -> p c b", c=GC),
                                        base, ALU.add).then_inc(group_taken, 1)

            def so_far(t, g):
                return h[:, g * GC:(g + 1) * GC, t * P:(t + 1) * P]

            def shift1_of(g):
                return t1t[:, g * GC:(g + 1) * GC].unsqueeze(2).to_broadcast([P, GC, P])

            def copy_shifts(half, k, g, banks):
                dve.wait_ge(spread_made, spreads(half, k, g))
                nc.vector.tensor_copy(shifts[:, :, g * GC:(g + 1) * GC],
                                      banks[g % len(banks)][:, :].rearrange("p (c d) -> p d c", c=GC)
                                      ).then_inc(spread_copied, 1)

            def output_tile(half, k, t, spread_next):
                if type(k) is int and k == 0:
                    dve.wait_ge(turn_made, turns(half, LAST_J, t, LAST_G))
                elif type(k) is int and k == LAST_J and t == LAST_T:
                    dve.wait_ge(group_taken, products(half, 1, k, 0, LAST_G) + MM_BANKS)
                else:
                    for p in range(PIECES):
                        dve.wait_ge(stored[t][p], stores(half, k, t) - 16)
                for g in range(GROUPS):
                    if t == 0:
                        dve.wait_ge(spread_copied, spreads(half, k, g))
                    dve.wait_ge(group_made, products(half, 1, k, t, g))
                    nc.vector.tensor_tensor(out_tile(half, k, t)[:, :, g * GC:(g + 1) * GC],
                                            mm_bank[g % MM_BANKS][:, :].rearrange("p (c d) -> p d c", c=GC),
                                            shifts[:, :, g * GC:(g + 1) * GC], ALU.add).then_inc(group_taken, 1)
                    if spread_next and g > 0:
                        dve.wait_ge(group_taken, products(half, 1, k, t, g - 1) + MM_BANKS)
                        copy_shifts(half, k + 1, g - 1, spread_bank2)
                if spread_next:
                    dve.wait_ge(group_taken, products(half, 1, k, t, LAST_G) + MM_BANKS)
                    copy_shifts(half, k + 1, LAST_G, spread_bank2)

            b, g_, be, m, v, y, w = prm1
            dve.wait_ge(params_loaded[0], 16 * 5)
            step(nc.vector.tensor_scalar(v, v, EPS, None, ALU.add))
            nc.vector.reciprocal(y, v).then_inc(root_asked, 1)
            dve.wait_ge(root_done, 1)
            step(nc.vector.tensor_tensor(w, y, y, ALU.mult))
            step(nc.vector.tensor_tensor(w, w, v, ALU.mult))
            step(nc.vector.tensor_scalar(w, w, -0.5, 1.5, ALU.mult, ALU.add))
            step(nc.vector.tensor_tensor(y, y, w, ALU.mult))
            step(nc.vector.tensor_tensor(g_, g_, y, ALU.mult))
            step(nc.vector.tensor_tensor(b, b, m, ALU.subtract))
            step(nc.vector.tensor_tensor(b, b, g_, ALU.mult))
            nc.vector.tensor_tensor(b, b, be, ALU.add).then_inc(bn1_worked, 1)
            dve.wait_ge(bn_turned, 1)
            nc.vector.tensor_copy(s1t[:, :], mm_bank[0][:, 0:C]).then_inc(bn1_ready, 1)
            nc.vector.tensor_copy(t1t[:, :], mm_bank[0][:, C:2 * C]).then_inc(bn1_ready, 1)
            dve.wait_ge(bn1_ready, 2)
            dve.sem_inc(group_taken, MM_BANKS)

            def layer2_step(n):
                b, g_, be, m, v, y, w = prm2
                if n == 0:
                    dve.wait_ge(params_loaded[1], 16 * 5 * CHUNKS)
                    step(nc.vector.tensor_scalar(v, v, EPS, None, ALU.add))
                elif n == 1:
                    nc.vector.reciprocal(y, v).then_inc(root_asked, 1)
                elif n == 2:
                    step(nc.vector.tensor_tensor(b, b, m, ALU.subtract))
                elif n == 3:
                    dve.wait_ge(root_done, 2)
                    step(nc.vector.tensor_tensor(w, y, y, ALU.mult))
                elif n == 4:
                    step(nc.vector.tensor_tensor(w, w, v, ALU.mult))
                elif n == 5:
                    step(nc.vector.tensor_scalar(w, w, -0.5, 1.5, ALU.mult, ALU.add))
                elif n == 6:
                    step(nc.vector.tensor_tensor(y, y, w, ALU.mult))
                elif n == 7:
                    step(nc.vector.tensor_tensor(g_, g_, y, ALU.mult))
                elif n == 8:
                    step(nc.vector.tensor_tensor(b, b, g_, ALU.mult))
                elif n == 9:
                    step(nc.vector.tensor_tensor(b, b, be, ALU.add))
                elif n - 10 < PARTS:
                    step(nc.vector.tensor_copy(part_bf[n - 10], b))
                    step(nc.vector.tensor_tensor(b, b, part_bf[n - 10], ALU.subtract))
                elif n == 10 + PARTS:
                    for part in range(PARTS):
                        rows = slice(part * PAIRS, (part + 1) * PAIRS)
                        for k in range(CHUNKS):
                            nc.vector.tensor_copy(t2p[rows, :, k * P:(k + 1) * P],
                                                  part_bf[part][k * PAIRS:(k + 1) * PAIRS].rearrange(
                                                      "p (two d) -> p two d", two=2))
                elif n == 11 + PARTS:
                    dve.wait_ge(ident_made, 2)
                    for part in range(PARTS):
                        rows = slice(part * PAIRS, (part + 1) * PAIRS)
                        last = nc.vector.tensor_copy(ones_at[rows], ident[rows, rows])
                    last.then_inc(bn2_worked, 1)

            assert GROUPS >= 12 + PARTS
            for half in range(HALVES):
                for t in range(TILES):
                    for g in range(GROUPS):
                        add_group(half, 0, t, g, shift1_of(g))
                        if half == 0 and t == LAST_T:
                            layer2_step(g)
                with dve.Fori(1, LAST_J) as j:
                    for t in range(TILES):
                        for g in range(GROUPS):
                            add_group(half, j, t, g, so_far(t, g))
                if half == 0:
                    dve.wait_ge(bn_turned, 2)
                    nc.vector.tensor_copy(s2t[:, :, :, :].rearrange("p k c two -> p two k c"),
                                          scale2_bank[:, 0:CHUNKS * C].rearrange(
                                              "p (two k c) -> p two k c", k=CHUNKS, two=2)
                                          ).then_inc(bn2_ready, 1)
                else:
                    for p in range(PIECES):
                        dve.wait_ge(last_stored[p], 16 * half)
                for t in range(TILES):
                    for g in range(GROUPS):
                        add_group(half, LAST_J, t, g, so_far(t, g))
                        if t == LAST_T:
                            copy_shifts(half, 0, g, spread_bank1)

                for t in range(TILES):
                    output_tile(half, 0, t, t == LAST_T)
                with dve.Fori(1, LAST_J) as k:
                    for t in range(TILES):
                        output_tile(half, k, t, t == LAST_T)
                for t in range(TILES):
                    output_tile(half, LAST_J, t, False)


_INS = ["r_x", "L0_rec_W1", "L0_rec_b1", "L0_rec_g1", "L0_rec_be1", "L0_rec_m1", "L0_rec_v1",
        "L0_rec_W2", "L0_rec_b2", "L0_rec_g2", "L0_rec_be2", "L0_rec_m2", "L0_rec_v2"]


def kernel(**inputs):
    import numpy as _np
    import concourse.bacc as _bacc
    from concourse import mybir as _mybir
    from concourse.bass_utils import run_bass_kernel_spmd as _run

    nc = _bacc.Bacc("TRN2", target_bir_lowering=False, num_devices=1, dynamic_dma_scratch_size=1024)
    arrays, args = {}, []
    for name in _INS:
        a = _np.ascontiguousarray(inputs[name])
        arrays[name] = a
        args.append(nc.dram_tensor(name, a.shape, _mybir.dt.from_np(a.dtype), kind="ExternalInput").ap())
    shape = inputs["r_x"].shape
    args.append(nc.dram_tensor("out", shape, _mybir.dt.float32, kind="ExternalOutput").ap())
    squeeze_expand_gate_kernel(nc, *args)
    return _run(nc, [arrays], core_ids=[0]).results[0]["out"]
```
